# Optimizing a Trainium2 kernel written in Bass

```python
import numpy as np
import jax
import jax.numpy as jnp

def _softmax(x, axis=-1):
    return jax.nn.softmax(x, axis=axis)

def _gelu(x):
    return jax.nn.gelu(x, approximate=True)

def _silu(x):
    return jax.nn.silu(x)

def _sigmoid(x):
    return jax.nn.sigmoid(x)

def _layernorm(x, axis=-1, eps=1e-05):
    m = jnp.mean(x, axis=axis, keepdims=True)
    v = jnp.var(x, axis=axis, keepdims=True)
    return (x - m) / jnp.sqrt(v + eps)

def _scatter_add(tgt, idx, src, axis=0):
    return tgt.at[idx].add(src)

def _segment_sum(src, seg, n):
    return jax.ops.segment_sum(src, seg, n)
kernel_name = 'mk_seq_preln_d1_jaxref_r8_28c167'

def setup_inputs(seed: int=0):
    np.random.seed(seed)
    _w = jnp.asarray

    def _L0_attn_setup():
        import jax, jax.numpy as jnp
        import numpy as np
        D_MODEL = 256
        D_INNER = 256
        D_XB = 64
        D_STATE = 32
        DT_RANK = 128
        D_FF = 704
        BATCH = 2
        SEQ = 128
        EPS = 1e-05

        def _rmsnorm(x, w):
            var = jnp.mean(jnp.square(x), axis=-1, keepdims=True)
            return x * jax.lax.rsqrt(var + EPS) * w

        def _selective_scan(x, dt, A, B, C):
            b, l, g, p = x.shape
            n = A.shape[-1]

            def step(h, inp):
                x_t, dt_t, B_t, C_t = inp
                dA = jnp.exp(dt_t[..., None] * A)
                h = dA * h + (dt_t * x_t)[..., None] * B_t[:, :, None, :]
                y = jnp.einsum('bgpn,bgn->bgp', h, C_t)
                return (h, y)
            h0 = jnp.zeros((b, g, p, n), x.dtype)
            xs = tuple((jnp.moveaxis(a, 1, 0) for a in (x, dt, B, C)))
            _, ys = jax.lax.scan(step, h0, xs)
            return jnp.moveaxis(ys, 0, 1)

        def _mamba(u, in_proj_w, dt_proj_w, dt_proj_b, A_log, D_param, out_proj_w):
            b, l, _ = u.shape
            zxbcdt = u @ in_proj_w.T
            splits = np.cumsum([D_INNER, D_XB, D_XB, D_INNER]).tolist()
            z, x, Bc, Cc, dt_raw = jnp.split(zxbcdt, splits, axis=-1)
            dt = jax.nn.softplus(dt_raw @ dt_proj_w.T + dt_proj_b)
            g = D_INNER // D_STATE
            g_kv = D_XB // D_STATE
            rep = g // g_kv
            x = jnp.repeat(x.reshape(b, l, g_kv, D_STATE), rep, axis=2)
            Bm = jnp.repeat(Bc.reshape(b, l, g_kv, D_STATE), rep, axis=2)
            Cm = Cc.reshape(b, l, g, D_STATE)
            A = -jnp.exp(A_log).reshape(g, D_STATE, D_STATE)
            dt = dt.reshape(b, l, g, D_STATE)
            y = _selective_scan(x, dt, A, Bm, Cm).reshape(b, l, D_INNER)
            y = y + x.reshape(b, l, D_INNER) * D_param
            y = y * jax.nn.silu(z)
            return y @ out_proj_w.T

        def _forward(hidden_states, in_proj_w, dt_proj_w, dt_proj_b, A_log, D_param, out_proj_w, gate_w, up_w, down_w, norm1_w, norm2_w):
            h = hidden_states + _mamba(_rmsnorm(hidden_states, norm1_w), in_proj_w, dt_proj_w, dt_proj_b, A_log, D_param, out_proj_w)
            xn = _rmsnorm(h, norm2_w)
            mlp = jax.nn.silu(xn @ gate_w.T) * (xn @ up_w.T) @ down_w.T
            return h + mlp
        key = jax.random.key(seed)
        ks = jax.random.split(key, 8)
        s = lambda k, shape, scale=0.02: jax.random.normal(k, shape, jnp.float32) * scale
        proj_dim = 2 * D_INNER + 2 * D_XB + DT_RANK
        return {'hidden_states': jax.random.normal(ks[0], (BATCH, SEQ, D_MODEL), jnp.float32), 'in_proj_w': s(ks[1], (proj_dim, D_MODEL)), 'dt_proj_w': s(ks[2], (D_INNER, DT_RANK)), 'dt_proj_b': jnp.full((D_INNER,), -4.6, jnp.float32), 'A_log': jnp.log(jnp.tile(jnp.arange(1, D_STATE + 1, dtype=jnp.float32), (D_INNER, 1))), 'D_param': jnp.ones((D_INNER,), jnp.float32), 'out_proj_w': s(ks[3], (D_MODEL, D_INNER)), 'gate_w': s(ks[4], (D_FF, D_MODEL)), 'up_w': s(ks[5], (D_FF, D_MODEL)), 'down_w': s(ks[6], (D_MODEL, D_FF)), 'norm1_w': jnp.ones((D_MODEL,), jnp.float32), 'norm2_w': jnp.ones((D_MODEL,), jnp.float32)}
    _L0_attn_in = _L0_attn_setup()

    def _L0_ffn_setup():
        import jax, jax.numpy as jnp
        import numpy as np
        B, S, D, H = (4, 256, 256, 1024)

        def fwht(x):
            orig_shape = x.shape
            n = orig_shape[-1]
            x = x.reshape(-1, n)
            h = 1
            while h < n:
                xb = x.reshape(-1, n // (2 * h), 2, h)
                a = xb[:, :, 0, :]
                b = xb[:, :, 1, :]
                x = jnp.stack([a + b, a - b], axis=2).reshape(-1, n)
                h *= 2
            scale = jnp.asarray(1.0 / np.sqrt(n), dtype=x.dtype)
            return (x * scale).reshape(orig_shape)
        key = jax.random.key(seed)
        kx, k1, k2, k3 = jax.random.split(key, 4)
        x = jax.random.normal(kx, (B, S, D), dtype=jnp.float32)
        W1 = jax.random.normal(k1, (H, D), dtype=jnp.float32) * (1.0 / np.sqrt(D))
        W2 = jax.random.normal(k2, (D, H), dtype=jnp.float32) * (1.0 / np.sqrt(H))
        W3 = jax.random.normal(k3, (H, D), dtype=jnp.float32) * (1.0 / np.sqrt(D))
        return {'x': x, 'W1': W1, 'W2': W2, 'W3': W3}
    _L0_ffn_in = _L0_ffn_setup()
    _d = {'L0_attn_hidden_states': _L0_attn_in['hidden_states'], 'L0_attn_in_proj_w': _L0_attn_in['in_proj_w'], 'L0_attn_dt_proj_w': _L0_attn_in['dt_proj_w'], 'L0_attn_dt_proj_b': _L0_attn_in['dt_proj_b'], 'L0_attn_A_log': _L0_attn_in['A_log'], 'L0_attn_D_param': _L0_attn_in['D_param'], 'L0_attn_out_proj_w': _L0_attn_in['out_proj_w'], 'L0_attn_gate_w': _L0_attn_in['gate_w'], 'L0_attn_up_w': _L0_attn_in['up_w'], 'L0_attn_down_w': _L0_attn_in['down_w'], 'L0_attn_norm1_w': _L0_attn_in['norm1_w'], 'L0_attn_norm2_w': _L0_attn_in['norm2_w'], 'L0_ffn_W1': _L0_ffn_in['W1'], 'L0_ffn_W2': _L0_ffn_in['W2'], 'L0_ffn_W3': _L0_ffn_in['W3']}
    _x0 = _d['L0_attn_hidden_states']
    _d['L0_attn_hidden_states'] = jax.random.normal(jax.random.fold_in(jax.random.key(seed), 1), (4, 1024, 256), dtype=_x0.dtype)
    del _x0
    return _d

def reference(L0_attn_hidden_states, L0_attn_in_proj_w, L0_attn_dt_proj_w, L0_attn_dt_proj_b, L0_attn_A_log, L0_attn_D_param, L0_attn_out_proj_w, L0_attn_gate_w, L0_attn_up_w, L0_attn_down_w, L0_attn_norm1_w, L0_attn_norm2_w, L0_ffn_W1, L0_ffn_W2, L0_ffn_W3):

    def _L0_attn_ref(hidden_states, in_proj_w, dt_proj_w, dt_proj_b, A_log, D_param, out_proj_w, gate_w, up_w, down_w, norm1_w, norm2_w):
        import jax, jax.numpy as jnp
        import numpy as np
        D_MODEL = 256
        D_INNER = 256
        D_XB = 64
        D_STATE = 32
        DT_RANK = 128
        D_FF = 704
        BATCH = 2
        SEQ = 128
        EPS = 1e-05

        def _rmsnorm(x, w):
            var = jnp.mean(jnp.square(x), axis=-1, keepdims=True)
            return x * jax.lax.rsqrt(var + EPS) * w

        def _selective_scan(x, dt, A, B, C):
            b, l, g, p = x.shape
            n = A.shape[-1]

            def step(h, inp):
                x_t, dt_t, B_t, C_t = inp
                dA = jnp.exp(dt_t[..., None] * A)
                h = dA * h + (dt_t * x_t)[..., None] * B_t[:, :, None, :]
                y = jnp.einsum('bgpn,bgn->bgp', h, C_t)
                return (h, y)
            h0 = jnp.zeros((b, g, p, n), x.dtype)
            xs = tuple((jnp.moveaxis(a, 1, 0) for a in (x, dt, B, C)))
            _, ys = jax.lax.scan(step, h0, xs)
            return jnp.moveaxis(ys, 0, 1)

        def _mamba(u, in_proj_w, dt_proj_w, dt_proj_b, A_log, D_param, out_proj_w):
            b, l, _ = u.shape
            zxbcdt = u @ in_proj_w.T
            splits = np.cumsum([D_INNER, D_XB, D_XB, D_INNER]).tolist()
            z, x, Bc, Cc, dt_raw = jnp.split(zxbcdt, splits, axis=-1)
            dt = jax.nn.softplus(dt_raw @ dt_proj_w.T + dt_proj_b)
            g = D_INNER // D_STATE
            g_kv = D_XB // D_STATE
            rep = g // g_kv
            x = jnp.repeat(x.reshape(b, l, g_kv, D_STATE), rep, axis=2)
            Bm = jnp.repeat(Bc.reshape(b, l, g_kv, D_STATE), rep, axis=2)
            Cm = Cc.reshape(b, l, g, D_STATE)
            A = -jnp.exp(A_log).reshape(g, D_STATE, D_STATE)
            dt = dt.reshape(b, l, g, D_STATE)
            y = _selective_scan(x, dt, A, Bm, Cm).reshape(b, l, D_INNER)
            y = y + x.reshape(b, l, D_INNER) * D_param
            y = y * jax.nn.silu(z)
            return y @ out_proj_w.T

        def _forward(hidden_states, in_proj_w, dt_proj_w, dt_proj_b, A_log, D_param, out_proj_w, gate_w, up_w, down_w, norm1_w, norm2_w):
            h = hidden_states + _mamba(_rmsnorm(hidden_states, norm1_w), in_proj_w, dt_proj_w, dt_proj_b, A_log, D_param, out_proj_w)
            xn = _rmsnorm(h, norm2_w)
            mlp = jax.nn.silu(xn @ gate_w.T) * (xn @ up_w.T) @ down_w.T
            return h + mlp
        return _forward(hidden_states, in_proj_w, dt_proj_w, dt_proj_b, A_log, D_param, out_proj_w, gate_w, up_w, down_w, norm1_w, norm2_w)

    def _L0_ffn_ref(x, W1, W2, W3):
        import jax, jax.numpy as jnp
        import numpy as np
        B, S, D, H = (4, 256, 256, 1024)

        def fwht(x):
            orig_shape = x.shape
            n = orig_shape[-1]
            x = x.reshape(-1, n)
            h = 1
            while h < n:
                xb = x.reshape(-1, n // (2 * h), 2, h)
                a = xb[:, :, 0, :]
                b = xb[:, :, 1, :]
                x = jnp.stack([a + b, a - b], axis=2).reshape(-1, n)
                h *= 2
            scale = jnp.asarray(1.0 / np.sqrt(n), dtype=x.dtype)
            return (x * scale).reshape(orig_shape)
        up_gate = jnp.einsum('bsd,hd->bsh', x, W1)
        up_lin = jnp.einsum('bsd,hd->bsh', x, W3)
        hidden = jax.nn.silu(up_gate) * up_lin
        hidden = fwht(hidden)
        out = jnp.einsum('bsh,dh->bsd', hidden, W2)
        return out
    x = L0_attn_hidden_states
    x = x + _L0_attn_ref(_layernorm(x, axis=-1), L0_attn_in_proj_w, L0_attn_dt_proj_w, L0_attn_dt_proj_b, L0_attn_A_log, L0_attn_D_param, L0_attn_out_proj_w, L0_attn_gate_w, L0_attn_up_w, L0_attn_down_w, L0_attn_norm1_w, L0_attn_norm2_w)
    x = x + _L0_ffn_ref(_layernorm(x, axis=-1), L0_ffn_W1, L0_ffn_W2, L0_ffn_W3)
    return x

_drawn_inputs = setup_inputs


def setup_inputs(seed=0):
    import zlib

    import numpy as np

    out = dict(_drawn_inputs(seed))
    spreads = {'L0_attn_dt_proj_b': (-4.599999904632568, 0.6),
     'L0_attn_D_param': (1.0, 0.6),
     'L0_attn_norm1_w': (1.0, 0.6),
     'L0_attn_norm2_w': (1.0, 0.6)}
    factors = {'L0_attn_in_proj_w': 5.19,
     'L0_attn_dt_proj_w': 8.0,
     'L0_attn_A_log': 8.0,
     'L0_attn_out_proj_w': 4.884,
     'L0_attn_gate_w': 21.813,
     'L0_attn_up_w': 19.537,
     'L0_attn_down_w': 19.649,
     'L0_ffn_W1': 8.0,
     'L0_ffn_W2': 8.0,
     'L0_ffn_W3': 8.0}
    for name, (base, spread) in spreads.items():
        noise = np.random.default_rng([zlib.crc32(name.encode()), seed]).standard_normal(out[name].shape)
        drawn = base * np.exp(spread * noise) if base else spread * noise
        out[name] = jnp.asarray(drawn.astype(out[name].dtype))
    for name, factor in factors.items():
        out[name] = (out[name] * factor).astype(out[name].dtype)
    return out
```

```python
from contextlib import ExitStack

import concourse.bass as bass
from concourse import mybir

F32 = mybir.dt.float32
F32R = mybir.dt.float32r
ALU = mybir.AluOpType
ACT = mybir.ActivationFunctionType

P = 128
D = 256
KD = D // P
SEQ = 1024
T = 512
SUB = T // P
TILES = 4 * SEQ // T
NS = 32
GH = 4
UH = 32
U = 2 * UH
FF = 704
GB = 5
H = 1024
HB = H // P
EPS = 1e-5
LAST = TILES - 1


def unit_channel(u):
    j = u % UH
    return 8 * (j % 4) + j // 4


PRE = {"uT", "dtr", "xb", "dtp0", "dtp1", "c0"}
MID = {"z", "c1"}
PLAN = ([("z", 0, 2, .86), ("c1", 0, 2, .86)]
        + [("out", k, 4, .43) for k in range(2)]
        + [("uT", k, 4, .11) for k in range(2)]
        + [("dtr", 0, 2, .86), ("xb", 0, 2, .86)]
        + [("hT", k, 4, .11) for k in range(2)]
        + [s for f in range(GB) for s in (("gate", f, 2, .86), ("up", f, 2, .86))] + [("gate", GB, 2, .86)]
        + [("down", k, 12, .43) for k in range(2)]
        + [("z", 1, 2, .86), ("c0", 0, 2, .86)]
        + [("xT", k, 4, .11) for k in range(2)]
        + [s for f in range(HB) for s in (("w1", f, 2, .86), ("w3", f, 2, .86))
           + ((("dtp0", 0, 1, .86),) if f == 1 else ())]
        + [("dtp1", 0, 1, .86)]
        + [("w2", k, 16, .43) for k in range(2)])
GAP = 5
AFTER = {("out", 0): (None, 4), ("hT", 0): (("out", 1), GAP), ("xT", 0): (("down", 1), GAP)}
RING = 3
FIRST_SLOT, LAST_SLOT = 0, 62
XL_SLOT = 4
SUM_COST = .9


def place_steps(rate):
    starts = [0.0]
    for u in range(U + 8):
        starts.append(starts[-1] + rate - SUM_COST * (u % 4 == 2))
    at, s, slots, ends = starts[FIRST_SLOT], FIRST_SLOT, {}, {}
    for q, (stage, k, n, c) in enumerate(PLAN):
        if (stage, k) in AFTER:
            before, gap = AFTER[stage, k]
            at = max(at, starts[ends.get(before, 0) + gap])
        for j in range(n):
            while at + 1e-6 >= starts[s + 1]:
                s += 1
            if s >= U:
                return None
            slots.setdefault(s, []).append((q, j))
            ends[stage, k] = s
            at += c
    return (slots, ends) if s <= LAST_SLOT else None


STEPS, ENDS = next(placed for placed in (place_steps(r / 100) for r in range(120, 300)) if placed)
USES = len(PLAN) + (-len(PLAN)) % RING
BANK = {step[:2]: q % RING for q, step in enumerate(PLAN)}


def build(nc, x, in_w, dt_w, dt_b, a_log, d_par, out_w, gu_w, down_w, n1, n2, w1, w3, w2, ident, pick, ysel, had, out):
    with ExitStack() as ctx:
        def sb(name, shape, dt=F32):
            return ctx.enter_context(nc.sbuf_tensor(name, shape, dt))

        def bank(name):
            return ctx.enter_context(nc.psum_tensor(name, [P, T], F32))

        def sem(name):
            return ctx.enter_context(nc.semaphore(name))

        in_s = sb("in_s", [P, KD, 6, P])
        dtw_s = sb("dtw_s", [P, 2, P])
        out_s = sb("out_s", [P, 2, D])
        gu_s = sb("gu_s", [P, KD, 2 * GB + 1, P])
        down_s = sb("down_s", [P, GB + 1, D])
        w1_s = sb("w1_s", [P, KD, H])
        w3_s = sb("w3_s", [P, KD, H])
        w2_s = sb("w2_s", [P, HB, D])
        ident_s = sb("ident_s", [P, P])
        pick_s = sb("pick_s", [P, 64 * NS], F32R)
        ysel_s = sb("ysel_s", [P, 60])
        an_s = sb("an_s", [P, U])
        par_s = sb("par_s", [P, 8])
        half_s = sb("half_s", [P, 8])
        kdt = sb("kdt", [P, 2, 2, T], F32R)
        kdx = sb("kdx", [P, 2, 2, T], F32R)
        b_s = sb("b_s", [P, 2, T])
        c_s = sb("c_s", [P, 2, T])
        xr_s = sb("xr_s", [P, 2, 2, T])
        zs_s = sb("zs_s", [P, 2, T])
        bt_s = sb("bt_s", [P, 4, T])
        h_s = sb("h_s", [P, 4, T])
        hc_s = sb("hc_s", [P, 8, T])
        carry = sb("carry", [P, U])
        yz_s = sb("yz_s", [P, 2, T])
        xin = sb("xin", [P, SUB, D])
        tok = sb("tok", [P, SUB, D])
        uT_s = sb("uT_s", [P, 2, KD, T])
        kept = sb("kept", [P, 2, 2, SUB])
        dtr_s = sb("dtr_s", [P, T])
        xb_s = sb("xb_s", [P, T])
        sp_e = sb("sp_e", [P, T])
        sp_l = sb("sp_l", [P, T])
        sp_r = sb("sp_r", [P, T])
        sp_w = sb("sp_w", [P, T])
        st_dt = sb("st_dt", [P, 2, T], F32R)
        st_dx = sb("st_dx", [P, 2, T], F32R)
        res = sb("res", [P, SUB, D])
        xo = sb("xo", [P, SUB, D])
        nT = sb("nT", [P, KD, T])
        th_s = sb("th_s", [P, 2, T])
        had_s = th_s[:, 0, 0:P]
        hd_s = sb("hd_s", [P, HB, T])
        m5_s = sb("m5_s", [P, T])
        bn = sb("bn", [P, 3, SUB, 6])
        mv = sb("mv", [P, 2, SUB, 2])
        ve = sb("ve", [P, 3, 8])
        rs = sb("rs", [P, 3, 8])
        nm = sb("nm", [P, 2, 8])
        mb = sb("mb", [P, 2, 8])
        sq = sb("sq", [P, SUB])

        p_dt = [bank(f"p_dt{k}") for k in range(2)]
        p_dx = [bank(f"p_dx{k}") for k in range(2)]
        p_y = bank("p_y")
        ring = [bank(f"p_r{k}") for k in range(RING)]

        l_w = {w: sem(f"l_{w}") for w in ("a", "b", "c", "d", "e")}
        l_x, l_xo, l_xrep, l_out = sem("l_x"), sem("l_xo"), sem("l_xrep"), sem("l_out")
        l_k = [sem(f"l_k{h}") for h in range(2)]
        l_b = [sem(f"l_b{h}") for h in range(2)]
        w_in, w_gu, w_out, w_an, w_zero, w_pick, w_had, w_w2, w_w2c = (
            sem(f"w_{n}") for n in ("in", "gu", "out", "an", "zero", "pick", "had", "w2", "w2c"))
        pe_dt, pe_dx, pe_y = sem("pe_dt"), sem("pe_dx"), sem("pe_y")
        mm = {s: sem(f"mm_{s}") for s in ("uT", "dtr", "xb", "dtp", "z", "c0", "c1", "out", "hT", "gate", "up", "down", "xT",
                                         "w1", "w3", "w2")}
        a_dA, a_u, a_uT, a_xl, a_dtr, a_xb = (sem(f"a_{n}") for n in ("dA", "u", "uT", "xl", "dtr", "xb"))
        a_c = [sem(f"a_c{h}") for h in range(2)]
        a_abs, a_rel, a_e, a_l, a_dth, a_dxh, a_zt = (sem(f"a_{n}") for n in
                                                     ("abs", "rel", "e", "l", "dth", "dxh", "zt"))
        a_sq, a_hn, a_hT, a_gt, a_xn, a_xT, a_ft, a_car = (sem(f"a_{n}") for n in
                                                          ("sq", "hn", "hT", "gt", "xn", "xT", "ft", "car"))
        v_bt, v_sc, v_st, v_mv, v_ve, v_zs, v_w, v_ln, v_c, v_dtl, v_dxl, v_kept = (sem(f"v_{n}") for n in
                                                               ("bt", "sc", "st", "mv", "ve", "zs", "w", "ln", "c", "dtl", "dxl", "kept"))
        v_yf, v_yz, v_h, v_ms, v_ga, v_mh, v_x1, v_st2, v_mv2, v_ve2 = (
            sem(f"v_{n}") for n in ("yf", "yz", "h", "ms", "ga", "mh", "x1", "st2", "mv2", "ve2"))
        v_fa, v_hd, v_o = sem("v_fa"), sem("v_hd"), sem("v_o")
        g_rr, g_rr2 = sem("g_rr"), sem("g_rr2")
        g_hc, g_r, g_r2, g_r3, g_s, g_dt, g_dx, g_hx = (sem(f"g_{n}") for n in
                                                            ("hc", "r", "r2", "r3", "s", "dt", "dx", "hx"))

        x_t = x.rearrange("b s d -> (b s) d")
        out_t = out.rearrange("b s d -> (b s) d")

        def rows(dram, t):
            return dram[bass.ds(t * T, T), :].rearrange("(s p) d -> p s d", p=P)

        def bodies(eng, body):
            body(-1, 1, True, False, False)
            body(0, 0, True, True, False)
            body(1, 1, True, True, True)
            with eng.Fori(1, LAST // 2) as pair:
                body(pair * 2, 0, True, True, True)
                body(pair * 2 + 1, 1, True, True, True)
            body(LAST - 1, 0, True, True, True)
            body(LAST, 1, False, True, True)
            body(LAST + 1, 0, False, False, True)

        def known(i):
            return isinstance(i, int)

        def from_tile(i, least):
            return not known(i) or i >= least

        block = ctx.enter_context(nc.Block())

        @block.sync
        def _(sp):
            sp.dma_start(par_s[:, 0:2], n1).then_inc(l_w["a"], 16)
            sp.dma_start(par_s[:, 2:4], n2).then_inc(l_w["a"], 16)
            sp.dma_start(par_s[:, 4:6], dt_b).then_inc(l_w["a"], 16)
            sp.dma_start(par_s[:, 6:8], d_par).then_inc(l_w["a"], 16)
            sp.dma_start(in_s[:, :, :, :], in_w).then_inc(l_w["b"], 16)
            sp.dma_start(ident_s[:, :], ident).then_inc(l_w["c"], 16)
            sp.dma_start(dtw_s[:, :, :], dt_w).then_inc(l_w["c"], 16)
            sp.dma_start(an_s[:, :], a_log).then_inc(l_w["c"], 16)
            sp.dma_start(hd_s[:, 0:4, :].rearrange("p a b -> p (a b)"), pick).then_inc(l_w["c"], 16)
            sp.dma_start(ysel_s[:, :], ysel).then_inc(l_w["c"], 16)

            sp.dma_start(xin[:, :, :], rows(x_t, 0)).then_inc(l_x, 16)

            def body(i, par, pre, units, post):
                nt = i + 1
                if known(i) and i == -1:
                    sp.dma_start(had_s, had).then_inc(l_w["d"], 16)
                    sp.wait_ge(w_pick, 1)
                    sp.dma_start(hd_s[:, 0:4, :].rearrange("p a (b d) -> p (a b) d", d=D), w2).then_inc(l_w["d"], 16)
                    sp.dma_start(out_s[:, :, :], out_w).then_inc(l_w["e"], 16)
                    sp.dma_start(gu_s[:, :, :, :], gu_w).then_inc(l_w["e"], 16)
                    sp.dma_start(down_s[:, 0:GB, :], down_w[:, 0:GB, :]).then_inc(l_w["e"], 16)
                    sp.dma_start(down_s[0:64, GB, :], down_w[0:64, GB, :]).then_inc(l_w["e"], 16)
                    sp.dma_start(w1_s[:, :, :], w1).then_inc(l_w["e"], 16)
                    sp.dma_start(w3_s[:, :, :], w3).then_inc(l_w["e"], 16)
                if post:
                    if from_tile(i - 1, 1):
                        sp.wait_ge(l_out, (i - 1) * 16)
                    sp.dma_start(xo[:, :, :], rows(x_t, i - 1)).then_inc(l_xo, 16)
                if pre:
                    sp.wait_ge(a_xb, nt + 1)
                    for h in range(2):
                        for g in range(GH):
                            sp.dma_start(xr_s[g:P:GH, 1 - par, h, :], xb_s[NS * h:NS * h + NS, :])\
                              .then_inc(l_xrep, 16)
                    for h in range(2):
                        if h == 1 and (not known(i) or nt < LAST):
                            sp.wait_ge(a_u, nt + 1)
                            sp.dma_start(xin[:, :, :], rows(x_t, nt + 1)).then_inc(l_x, 16)
                        if units:
                            sp.wait_ge(v_bt, i * U + UH * (h + 1))
                        for g in range(GH):
                            sp.dma_start(b_s[NS * g:NS * g + NS, h, :], xb_s[64 + NS * h:96 + NS * h, :])\
                              .then_inc(l_b[h], 16)
                        sp.wait_ge(a_dth, nt * 2 + h + 1)
                        sp.wait_ge(v_dtl, nt * 2 + h + 1)
                        sp.wait_ge(a_dxh, nt * 2 + h + 1)
                        sp.wait_ge(v_dxl, nt * 2 + h + 1)
                        if units:
                            sp.wait_ge(pe_dt, i * U + UH * (h + 1))
                        for k, st in ((kdt, st_dt), (kdx, st_dx)):
                            for part in range(2):
                                for q in range(2):
                                    sp.dma_start(k[64 * part:64 * part + 64, h, q, :].bitcast(F32),
                                                 st[64 * q:64 * q + 64, part, :].bitcast(F32)).then_inc(l_k[h], 16)

            bodies(sp, body)
            sp.wait_ge(l_out, 16 * TILES)

        @block.tensor
        def _(pe):
            freed = {"uT": (a_uT, 2), "dtr": (a_dtr, 1), "xb": (a_xb, 1), "dtp0": (a_rel, 2), "dtp1": (a_rel, 2),
                     "z": (v_zs, 2), "c0": (a_c[0], 1), "c1": (a_c[1], 1), "out": (v_h, 2), "hT": (a_hT, 2), "gate": (v_ga, GB + 1),
                     "up": (v_mh, GB + 1), "down": (v_x1, 2), "xT": (a_xT, 2), "w1": (v_fa, HB), "w3": (v_hd, HB),
                     "w2": (v_o, 2)}

            def done(stage, k, tile):
                s, per = freed[stage]
                k = {"dtp1": 1}.get(stage, k)
                if (stage, k) == ("gate", GB):
                    s = v_mh
                pe.wait_ge(s, tile * per + k + 1)

            def tile_of(stage, i):
                return i + 1 if stage in PRE else i if stage in MID else i - 1

            def bank_free(q, i, on):
                r = q - RING
                while r >= 0 and not on(PLAN[r][0]):
                    r -= RING
                if r >= 0:
                    stage, k = PLAN[r][:2]
                    done(stage, k, tile_of(stage, i))
                    return
                uses = range(q % RING, len(PLAN), RING)
                if not known(i) or 0 <= i <= LAST:
                    stage, k = [PLAN[p] for p in uses if PLAN[p][0] in PRE][-1][:2]
                    done(stage, k, i)
                if from_tile(i, 2):
                    stage = [PLAN[p] for p in uses if PLAN[p][0] not in PRE | MID][-1][0]
                    s, per = freed[stage]
                    pe.wait_ge(s, (i - 1) * per)

            def spread(i, u):
                h, p = u // UH, unit_channel(u)
                n = i * U + u
                sel = pick_s[:, P * (p % 16):P * (p % 16) + P]
                if u % UH == 0:
                    pe.wait_ge(l_k[h], (i + 1) * 128)
                if u >= 2 or from_tile(i, 1):
                    pe.wait_ge(v_bt, n - 1)
                nc.tensor.matmul(p_dx[u % 2][:, :], sel, kdx[:, h, p // 16, :], start=True, stop=True)\
                    .then_inc(pe_dx, 1)
                if u >= 2 or from_tile(i, 1):
                    pe.wait_ge(v_sc, n - 1)
                nc.tensor.matmul(p_dt[u % 2][:, :], sel, kdt[:, h, p // 16, :], start=True, stop=True)\
                    .then_inc(pe_dt, 1)

            def sum_states(i, m):
                pe.wait_ge(g_hc, i * U + 4 * m + 4)
                if m % 8 == 0 and (m or from_tile(i, 1)):
                    pe.wait_ge(v_yf, i * 2 + m // 8)
                for j in range(4):
                    u = 4 * m + j
                    row = unit_channel(u) % 8
                    last = nc.tensor.matmul(p_y[32 * j:32 * j + 32, :], ysel_s[:, 28 - 4 * row:60 - 4 * row],
                                            hc_s[:, u % 8, :], start=(m % 8 == 0), stop=(m % 8 == 7))
                last.then_inc(pe_y, 1)

            def dense(q, j, i, par, on):
                stage, k, n, _ = PLAN[q]
                t = tile_of(stage, i)
                ps = ring[q % RING]
                if j == 0:
                    bank_free(q, i, on)
                if stage in ("uT", "hT", "xT"):
                    src, ready = {"uT": (a_u, 1), "hT": (a_hn, 1), "xT": (a_xn, 1)}[stage]
                    if j == 0:
                        pe.wait_ge(src, t + 1)
                    ins = nc.tensor.transpose(ps[:, P * j:P * j + P], tok[:, j, P * k:P * k + P], ident_s[:, :])
                elif stage in ("dtr", "xb", "c0", "c1", "z"):
                    blk = {"dtr": 0, "xb": 1, "c0": 2, "c1": 3, "z": 4}[stage] + k
                    pe.wait_ge(a_uT, t * 2 + j + 1)
                    u_par = 1 - par if stage in PRE else par
                    ins = nc.tensor.matmul(ps[:, :], in_s[:, j, blk, :], uT_s[:, u_par, j, :],
                                           start=(j == 0), stop=(j == 1))
                elif stage in ("dtp0", "dtp1"):
                    pe.wait_ge(a_dtr, t + 1)
                    ins = nc.tensor.matmul(ps[:, :], dtw_s[:, int(stage[3]), :], dtr_s[:, :], start=True, stop=True)
                elif stage == "out":
                    s, c = 2 * k + j // 2, j % 2
                    if j == 0:
                        pe.wait_ge(v_yz, t * 2 + 2)
                    ins = nc.tensor.matmul(ps[:, D * (j // 2):D * (j // 2) + D], yz_s[:, c, P * s:P * s + P],
                                           out_s[:, c, :], start=(c == 0), stop=(c == 1))
                elif stage in ("gate", "up"):
                    blk = 2 * k + (stage == "up")
                    pe.wait_ge(a_hT, t * 2 + j + 1)
                    ins = nc.tensor.matmul(ps[:, :], gu_s[:, j, blk, :], nT[:, j, :], start=(j == 0), stop=(j == 1))
                elif stage == "down":
                    s, f = 2 * k + j // 6, j % 6
                    if k == 0:
                        pe.wait_ge(v_mh, t * 6 + f + 1)
                    src = m5_s[:, P * s:P * s + P] if f == GB else hd_s[:, f, P * s:P * s + P]
                    ins = nc.tensor.matmul(ps[:, D * (j // 6):D * (j // 6) + D], src, down_s[:, f, :],
                                           start=(f == 0), stop=(f == GB))
                elif stage in ("w1", "w3"):
                    w = w1_s if stage == "w1" else w3_s
                    pe.wait_ge(a_xT, t * 2 + j + 1)
                    ins = nc.tensor.matmul(ps[:, :], w[:, j, P * k:P * k + P], nT[:, j, :],
                                           start=(j == 0), stop=(j == 1))
                else:
                    s, f = 2 * k + j // 8, j % 8
                    if k == 0:
                        pe.wait_ge(v_hd, t * 8 + f + 1)
                    ins = nc.tensor.matmul(ps[:, D * (j // 8):D * (j // 8) + D], hd_s[:, f, P * s:P * s + P],
                                           w2_s[:, f, :], start=(f == 0), stop=(f == HB - 1))
                if j == n - 1:
                    ins.then_inc(mm[stage[:3] if stage[:3] == "dtp" else stage], 1)

            def transform_w2():
                pe.wait_ge(w_had, 6)
                pe.wait_ge(a_c[0], 1)
                pe.wait_ge(a_rel, 2)
                for k in range(4):
                    ps = ring[k] if k < RING else p_y
                    nc.tensor.matmul(ps[:, :], had_s, hd_s[:, 4 + k, :], start=True, stop=True).then_inc(w_w2, 1)

            def body(i, par, pre, units, post):
                def on(stage):
                    return pre if stage in PRE else units if stage in MID else post

                for u in range(U):
                    if known(i) and i == -1 and u == ENDS["dtp1", 0] + 1:
                        transform_w2()
                    if known(i) and i == 0 and u == 0:
                        pe.wait_ge(w_w2c, 4)
                        pe.wait_ge(w_out, 2)
                        pe.wait_ge(w_gu, 2)
                        pe.wait_ge(w_zero, 3)
                    if (units if u + 2 < U else pre):
                        spread(i + (u + 2) // U, (u + 2) % U)
                    if u == 2 and post:
                        sum_states(i - 1, 15)
                    if units and u >= 6 and (u - 6) % 4 == 0:
                        sum_states(i, (u - 6) // 4)
                    for q, j in STEPS.get(u, []):
                        if on(PLAN[q][0]):
                            dense(q, j, i, par, on)
            pe.wait_ge(w_pick, 1)
            pe.wait_ge(w_in, 2)
            pe.wait_ge(l_w["c"], 80)
            bodies(pe, body)

        @block.scalar
        def _(act):
            A = nc.scalar.activation

            act.wait_ge(l_w["a"], 64)
            act.wait_ge(l_w["b"], 16)
            for k in range(KD):
                A(in_s[:, k, :, :], in_s[:, k, :, :], ACT.Copy, scale=par_s[:, k:k + 1]).then_inc(w_in, 1)
            act.wait_ge(l_w["c"], 80)
            A(an_s[:, :], an_s[:, :], ACT.Exp).then_inc(w_an, 1)
            act.wait_ge(w_an, 1)
            A(an_s[:, :], an_s[:, :], ACT.Copy, scale=-1.0).then_inc(w_an, 1)
            act.wait_ge(w_an, 2)

            def scale_weights():
                act.wait_ge(l_w["e"], 96)
                act.wait_ge(w_zero, 3)
                A(out_s[:, :, :], out_s[:, :, :], ACT.Copy, scale=0.5).then_inc(w_out, 1)
                A(down_s[:, :, :], down_s[:, :, :], ACT.Copy, scale=0.5).then_inc(w_out, 1)
                for k in range(KD):
                    A(gu_s[:, k, :, :], gu_s[:, k, :, :], ACT.Copy, scale=par_s[:, 2 + k:3 + k]).then_inc(w_gu, 1)

            def keep_w2():
                for k in range(4):
                    act.wait_ge(w_w2, k + 1)
                    src = (ring[k] if k < RING else p_y)[:, :].rearrange("p (b d) -> p b d", d=D)
                    A(w2_s[:, 2 * k:2 * k + 2, :], src, ACT.Copy).then_inc(w_w2c, 1)

            def decay(i, u):
                act.wait_ge(pe_dt, i * U + u + 1)
                c = UH * (u // UH) + unit_channel(u)
                A(p_dt[u % 2][:, :], p_dt[u % 2][:, :], ACT.Exp, scale=an_s[:, c:c + 1]).then_inc(a_dA, 1)

            def keep_states(i, u):
                act.wait_ge(v_sc, i * U + u + 2)
                A(carry[:, u:u + 2], h_s[:, u % 4:u % 4 + 2, T - 1], ACT.Copy).then_inc(a_car, 1)

            def normalise(dst, src, scale, bias, signal):
                for s in range(SUB):
                    if bias is None:
                        ins = A(dst[:, s, :], src[:, s, :], ACT.Copy, scale=scale[:, s:s + 1])
                    else:
                        ins = A(dst[:, s, :], src[:, s, :], ACT.Identity, scale=scale[:, s:s + 1],
                                bias=bias[:, s:s + 1])
                ins.then_inc(signal, 1)

            def softplus(t, u, h):
                s0 = ENDS[f"dtp{h}", 0]
                m = t * 2 + h
                if u == s0 + 1:
                    act.wait_ge(mm["dtp"], m + 1)
                    if h or from_tile(t, 1):
                        act.wait_ge(v_c, m)
                        act.wait_ge(g_dt, m)
                    v = ring[BANK[f"dtp{h}", 0]][:, :]
                    A(sp_e[:, :], v, ACT.Abs, bias=par_s[:, 4 + h:5 + h]).then_inc(a_abs, 1)
                    A(sp_r[:, :], v, ACT.Relu, bias=par_s[:, 4 + h:5 + h]).then_inc(a_rel, 1)
                    act.wait_ge(a_abs, m + 1)
                    A(sp_e[:, :], sp_e[:, :], ACT.Exp, scale=-1.0).then_inc(a_e, 1)
                if u == s0 + 3:
                    act.wait_ge(v_w, m + 1)
                    if h or from_tile(t, 1):
                        act.wait_ge(v_dtl, m)
                    A(sp_l[:, :], sp_w[:, :], ACT.Ln).then_inc(a_l, 1)
                if u == s0 + 8:
                    if h:
                        act.wait_ge(l_k[0], (t + 1) * 128)
                    elif from_tile(t, 1):
                        act.wait_ge(l_k[1], t * 128)
                    act.wait_ge(g_dt, m + 1)
                    A(st_dt[:, 0, :], sp_l[:, :], ACT.Copy).then_inc(a_dth, 1)
                    act.wait_ge(g_dx, m + 1)
                    A(st_dx[:, 0, :], sp_w[:, :], ACT.Copy).then_inc(a_dxh, 1)

            def body(i, par, pre, units, post):
                nt, pt, other = i + 1, i - 1, 1 - par
                for u in range(U):
                    if known(i) and i == -1 and u == ENDS["dtp0", 0] + 5:
                        scale_weights()
                    if known(i) and i == -1 and u == ENDS["dtp1", 0] + 5:
                        keep_w2()
                    if (units if u + 1 < U else pre):
                        decay(i + (u + 1) // U, (u + 1) % U)
                    if units and par == 0 and u >= 2 and u % 2 == 0:
                        keep_states(i, u - 2)
                    if units:
                        for k in range(2):
                            if u == ENDS["z", k] + 1:
                                act.wait_ge(mm["z"], i * 2 + k + 1)
                                if from_tile(i, 1):
                                    act.wait_ge(v_yz, i * 2 - 1 + k)
                                A(zs_s[:, k, :], ring[BANK["z", k]][:, :], ACT.Tanh, scale=0.5).then_inc(a_zt, 1)
                        if u == ENDS["c1", 0] + 1:
                            act.wait_ge(mm["c1"], i + 1)
                            if from_tile(i, 1):
                                act.wait_ge(g_hc, i * U)
                            A(c_s[:, 1, :], ring[BANK["c1", 0]][:, :], ACT.Copy).then_inc(a_c[1], 1)
                    if pre:
                        if u == 3:
                            act.wait_ge(g_r, nt + 1)
                            act.wait_ge(l_x, (nt + 1) * 16)
                            if post:
                                act.wait_ge(mm["xT"], pt * 2)
                            if from_tile(nt, 1):
                                act.wait_ge(mm["uT"], nt * 2)
                            normalise(tok, xin, rs[:, 0, SUB:], mb[:, 0, SUB:], a_u)
                        for k in range(2):
                            if u == ENDS["uT", k] + 1:
                                act.wait_ge(mm["uT"], nt * 2 + k + 1)
                                if from_tile(i, 1):
                                    act.wait_ge(mm["z"], i * 2)
                                A(uT_s[:, other, k, :], ring[BANK["uT", k]][:, :], ACT.Copy).then_inc(a_uT, 1)
                        if u == ENDS["c0", 0] + 1:
                            act.wait_ge(mm["c0"], nt + 1)
                            if units:
                                act.wait_ge(g_hc, i * U + UH)
                            A(c_s[:, 0, :], ring[BANK["c0", 0]][:, :], ACT.Copy).then_inc(a_c[0], 1)
                        if u == ENDS["dtr", 0] + 1:
                            act.wait_ge(mm["dtr"], nt + 1)
                            if from_tile(nt, 1):
                                act.wait_ge(mm["dtp"], nt * 2)
                            A(dtr_s[:, :], ring[BANK["dtr", 0]][:, :], ACT.Copy).then_inc(a_dtr, 1)
                        if u == ENDS["xb", 0] + 1:
                            act.wait_ge(mm["xb"], nt + 1)
                            if from_tile(nt, 1):
                                act.wait_ge(l_xrep, nt * 128)
                                act.wait_ge(l_b[0], nt * 64)
                                act.wait_ge(l_b[1], nt * 64)
                            A(xb_s[:, :], ring[BANK["xb", 0]][:, :], ACT.Copy).then_inc(a_xb, 1)
                        for h in range(2):
                            softplus(nt, u, h)
                    if post:
                        if u == XL_SLOT:
                            act.wait_ge(l_xo, (pt + 1) * 16)
                            act.wait_ge(v_kept, pt + 1)
                            if from_tile(pt, 1):
                                act.wait_ge(a_xn, pt)
                                act.wait_ge(v_o, pt * 2)
                            normalise(res, xo, kept[:, other, 0, :], kept[:, other, 1, :], a_xl)
                        for k in range(2):
                            if u == ENDS["out", k] + 1:
                                act.wait_ge(v_h, pt * 2 + k + 1)
                                if k == 0 and from_tile(pt, 1):
                                    act.wait_ge(v_hd, pt * HB)
                                for s in (2 * k, 2 * k + 1):
                                    ins = A(th_s[:, s // 2, D * (s % 2):D * (s % 2) + D], res[:, s, :], ACT.Square,
                                            accum_out=sq[:, s:s + 1])
                                ins.then_inc(a_sq, 1)
                    if post:
                        if u == ENDS["out", 1] + 3:
                            act.wait_ge(g_r2, pt + 1)
                            if pre:
                                act.wait_ge(mm["uT"], nt * 2 + 2)
                            normalise(tok, res, rs[:, 1, :], None, a_hn)
                        for k in range(2):
                            if u == ENDS["hT", k] + 1:
                                act.wait_ge(mm["hT"], pt * 2 + k + 1)
                                if from_tile(pt, 1):
                                    act.wait_ge(mm["w3"], pt * HB)
                                A(nT[:, k, :], ring[BANK["hT", k]][:, :], ACT.Copy).then_inc(a_hT, 1)
                            if u == ENDS["xT", k] + 1:
                                act.wait_ge(mm["xT"], pt * 2 + k + 1)
                                act.wait_ge(mm["gate"], (pt + 1) * (GB + 1))
                                A(nT[:, k, :], ring[BANK["xT", k]][:, :], ACT.Copy).then_inc(a_xT, 1)
                        for f in range(GB + 1):
                            if u == ENDS["gate", f] + 1:
                                act.wait_ge(mm["gate"], pt * (GB + 1) + f + 1)
                                if f >= 2:
                                    act.wait_ge(v_mh, pt * (GB + 1) + f - 1)
                                elif from_tile(pt, 1):
                                    act.wait_ge(v_hd, pt * HB)
                                n = 64 if f == GB else P
                                A(th_s[0:n, f % 2, :], ring[BANK["gate", f]][0:n, :], ACT.Tanh, scale=0.5)\
                                    .then_inc(a_gt, 1)
                        if u == ENDS["down", 1] + 2:
                            act.wait_ge(g_r3, pt + 1)
                            act.wait_ge(mm["hT"], pt * 2 + 2)
                            normalise(tok, res, rs[:, 2, :], mb[:, 1, :], a_xn)
                        for f in range(HB):
                            if u == ENDS["w1", f] + 1:
                                act.wait_ge(mm["w1"], pt * HB + f + 1)
                                if f >= 2:
                                    act.wait_ge(v_hd, pt * HB + f - 1)
                                else:
                                    act.wait_ge(v_mh, (pt + 1) * (GB + 1))
                                A(th_s[:, f % 2, :], ring[BANK["w1", f]][:, :], ACT.Tanh, scale=0.5)\
                                    .then_inc(a_ft, 1)
                if units and par == 0:
                    keep_states(i, U - 2)

            bodies(act, body)

        @block.vector
        def _(dve):
            V = nc.vector

            V.memset(half_s[:, :], -0.5).then_inc(w_zero, 1)
            V.memset(m5_s[:, :], 0.0).then_inc(w_zero, 1)
            V.memset(down_s[64:P, GB, :], 0.0).then_inc(w_zero, 1)
            dve.wait_ge(w_zero, 3)
            dve.wait_ge(l_w["c"], 80)
            V.tensor_copy(pick_s[:, :], hd_s[:, 0:4, :].rearrange("p a b -> p (a b)")).then_inc(w_pick, 1)

            def butterflies():
                dve.wait_ge(l_w["d"], 32)
                for n, d in enumerate((4, 2, 1)):
                    if n:
                        dve.wait_ge(w_had, 2 * n)
                    a, b = (0, 4) if n % 2 == 0 else (4, 0)
                    src, dst = (hd_s[:, o:o + 4, :].rearrange("p a (b c) -> p (a b c)", c=D)
                                .rearrange("p (o two e) -> p o two e", two=2, e=d * D) for o in (a, b))
                    V.tensor_tensor(dst[:, :, 0, :], src[:, :, 0, :], src[:, :, 1, :], ALU.add).then_inc(w_had, 1)
                    V.tensor_tensor(dst[:, :, 1, :], src[:, :, 0, :], src[:, :, 1, :], ALU.subtract)\
                        .then_inc(w_had, 1)

            def drive(i, u):
                h = u // UH
                n = i * U + u
                if u % UH == 0:
                    dve.wait_ge(l_b[h], (i + 1) * 64)
                dve.wait_ge(pe_dx, n + 1)
                if u >= 4 or from_tile(i, 1):
                    dve.wait_ge(v_sc, n - 3)
                V.tensor_tensor(bt_s[:, u % 4, :], p_dx[u % 2][:, :], b_s[:, h, :], ALU.mult)\
                    .then_inc(v_bt, 1)

            def scan(i, par, u):
                n = i * U + u
                dve.wait_ge(a_dA, n + 1)
                dve.wait_ge(v_bt, n + 1)
                if u >= 4 or from_tile(i, 1):
                    dve.wait_ge(g_hc, n - 3)
                if par == 0 and u >= 4:
                    dve.wait_ge(a_car, i * (UH // 2) + (u - 4) // 2 + 1)
                if par:
                    dve.wait_ge(a_car, (i - 1) * (UH // 2) + max(u // 2 + 1, UH if u < 4 else 0))
                V.tensor_tensor_scan(h_s[:, u % 4, :], p_dt[u % 2][:, :], bt_s[:, u % 4, :],
                                     carry[:, u:u + 1] if par else 0.0, ALU.mult, ALU.add).then_inc(v_sc, 1)

            def gate_y(t, par, h):
                m = t * 2 + h
                dve.wait_ge(pe_y, t * (U // 4) + 8 * h + 8)
                if from_tile(t, 1):
                    dve.wait_ge(mm["out"], t * 2)
                V.scalar_tensor_tensor(out=yz_s[:, h, :], in0=xr_s[:, par, h, :], scalar=par_s[:, 6 + h:7 + h],
                                       in1=p_y[:, :], op0=ALU.mult, op1=ALU.add).then_inc(v_yf, 1)

            def gate_z(t, par, h):
                dve.wait_ge(v_yf, t * 2 + h + 1)
                dve.wait_ge(v_zs, t * 2 + h + 1)
                V.tensor_tensor(yz_s[:, h, :], yz_s[:, h, :], zs_s[:, h, :], ALU.mult).then_inc(v_yz, 1)

            def body(i, par, pre, units, post):
                nt, pt, other = i + 1, i - 1, 1 - par
                for u in range(U):
                    if known(i) and i == -1 and u == ENDS["dtr", 0]:
                        butterflies()
                    if (units if u + 1 < U else pre):
                        drive(i + (u + 1) // U, (u + 1) % U)
                    if units:
                        scan(i, par, u)
                    if post and u == 3:
                        gate_y(pt, other, 1)
                        gate_z(pt, other, 1)
                    if units:
                        for k in range(2):
                            if u == ENDS["z", k] + 2:
                                dve.wait_ge(a_zt, i * 2 + k + 1)
                                V.scalar_tensor_tensor(out=zs_s[:, k, :], in0=zs_s[:, k, :], scalar=1.0,
                                                       in1=ring[BANK["z", k]][:, :], op0=ALU.add, op1=ALU.mult)\
                                    .then_inc(v_zs, 1)
                    if pre:
                        if u < 2:
                            if u == 0:
                                dve.wait_ge(l_x, (nt + 1) * 16)
                            if from_tile(nt, 1):
                                dve.wait_ge(v_ve, nt)
                            for s in (2 * u, 2 * u + 1):
                                V.bn_stats(bn[:, 0, s, :], xin[:, s, :]).then_inc(v_st, 1)
                        if u == 1:
                            dve.wait_ge(v_st, nt * 4 + 4)
                            V.tensor_copy(nm[:, 1, 4:5], half_s[:, 0:1])
                            for s in range(SUB):
                                V.bn_aggr(mv[:, 0, s, :], bn[:, 0, s, :]).then_inc(v_mv, 1)
                            dve.wait_ge(v_mv, nt * 4 + 4)
                            if from_tile(nt, 1):
                                dve.wait_ge(g_r, nt)
                            V.tensor_scalar(ve[:, 0, 0:SUB], mv[:, 0, :, 1], EPS, None, ALU.add)
                            V.tensor_scalar(ve[:, 0, SUB:], mv[:, 0, :, 1], 1.0 + EPS, EPS * EPS, ALU.mult, ALU.add)
                            V.tensor_scalar(nm[:, 0, 0:SUB], mv[:, 0, :, 0], -1.0, None, ALU.mult)
                            V.tensor_scalar(nm[:, 0, SUB:], mv[:, 0, :, 0], -1.0, None, ALU.mult).then_inc(v_ve, 1)
                        if u == XL_SLOT + 1:
                            dve.wait_ge(g_r, nt + 1)
                            if post:
                                dve.wait_ge(a_xl, i)
                            V.tensor_copy(kept[:, other, 0, :], rs[:, 0, 0:SUB])
                            V.tensor_copy(kept[:, other, 1, :], mb[:, 0, 0:SUB]).then_inc(v_kept, 1)
                        for h in range(2):
                            s0, m = ENDS[f"dtp{h}", 0], nt * 2 + h
                            if u == s0 + 2:
                                dve.wait_ge(a_e, m + 1)
                                if h or from_tile(nt, 1):
                                    dve.wait_ge(a_dxh, m)
                                    dve.wait_ge(v_dxl, m)
                                V.tensor_scalar(sp_w[:, :], sp_e[:, :], 1.0, None, ALU.add).then_inc(v_w, 1)
                            if u == s0 + 4:
                                dve.wait_ge(a_l, m + 1)
                                V.scalar_tensor_tensor(out=sp_l[:, :], in0=sp_w[:, :], scalar=-1.0, in1=sp_l[:, :],
                                                       op0=ALU.add, op1=ALU.min).then_inc(v_ln, 1)
                                dve.wait_ge(v_ln, m + 1)
                                V.scalar_tensor_tensor(out=sp_w[:, :], in0=sp_w[:, :], scalar=-1.0, in1=sp_e[:, :],
                                                       op0=ALU.add, op1=ALU.subtract).then_inc(v_c, 1)
                            if u == s0 + 9:
                                if h:
                                    dve.wait_ge(l_k[0], (nt + 1) * 128)
                                elif from_tile(nt, 1):
                                    dve.wait_ge(l_k[1], nt * 128)
                                dve.wait_ge(a_dth, m + 1)
                                V.tensor_tensor(st_dt[:, 1, :], sp_l[:, :], st_dt[:, 0, :].bitcast(F32), ALU.subtract)\
                                    .then_inc(v_dtl, 1)
                                dve.wait_ge(a_dxh, m + 1)
                                V.tensor_tensor(st_dx[:, 1, :], sp_w[:, :], st_dx[:, 0, :].bitcast(F32), ALU.subtract)\
                                    .then_inc(v_dxl, 1)
                    if units and u == 36:
                        gate_y(i, par, 0)
                    if units and u == 37:
                        gate_z(i, par, 0)
                    if post:
                        for k in range(2):
                            two = slice(2 * k, 2 * k + 2)

                            def view(stage):
                                return ring[BANK[stage, k]][:, :].rearrange("p (s d) -> p s d", d=D)

                            if u == ENDS["out", k] + 1:
                                dve.wait_ge(mm["out"], pt * 2 + k + 1)
                                dve.wait_ge(a_xl, pt + 1)
                                V.tensor_tensor(res[:, two, :], view("out"), res[:, two, :], ALU.add)\
                                    .then_inc(v_h, 1)
                            if u == ENDS["down", k] + 1:
                                dve.wait_ge(mm["down"], pt * 2 + k + 1)
                                dve.wait_ge(g_hx, pt * 2 + k + 1)
                                V.tensor_tensor(res[:, two, :], view("down"), res[:, two, :], ALU.add)\
                                    .then_inc(v_x1, 1)
                                dve.wait_ge(v_x1, pt * 2 + k + 1)
                                for s in (2 * k, 2 * k + 1):
                                    V.bn_stats(bn[:, 1, s, :], res[:, s, :]).then_inc(v_st2, 1)
                                if k == 1:
                                    dve.wait_ge(v_st2, pt * 4 + 4)
                                    V.tensor_copy(nm[:, 1, 5:6], half_s[:, 0:1])
                                    for s in range(SUB):
                                        V.bn_aggr(mv[:, 1, s, :], bn[:, 1, s, :]).then_inc(v_mv2, 1)
                            if u == min(ENDS["w2", k] + 2, U - 1):
                                dve.wait_ge(mm["w2"], pt * 2 + k + 1)
                                dve.wait_ge(g_hx, pt * 2 + 2)
                                V.tensor_tensor(xo[:, two, :], view("w2"), res[:, two, :], ALU.add)\
                                    .then_inc(v_o, 1)
                        if u == ENDS["out", 1] + 2:
                            dve.wait_ge(a_sq, pt * 2 + 2)
                            if from_tile(pt, 1):
                                dve.wait_ge(g_r2, pt)
                            V.tensor_scalar(ve[:, 1, 0:SUB], sq[:, :], 1.0 / D, EPS, ALU.mult, ALU.add)\
                                .then_inc(v_ms, 1)
                        if u == ENDS["down", 1] + 1:
                            dve.wait_ge(v_mv2, pt * 4 + 4)
                            if from_tile(pt, 1):
                                dve.wait_ge(g_r3, pt)
                            V.tensor_scalar(ve[:, 2, 0:SUB], mv[:, 1, :, 1], EPS, None, ALU.add)
                            V.tensor_scalar(nm[:, 1, 0:SUB], mv[:, 1, :, 0], -1.0, None, ALU.mult).then_inc(v_ve2, 1)
                        for f in range(GB + 1):
                            m = pt * (GB + 1) + f
                            n = 64 if f == GB else P
                            if u == ENDS["gate", f] + 2:
                                dve.wait_ge(a_gt, m + 1)
                                V.scalar_tensor_tensor(out=th_s[0:n, f % 2, :], in0=th_s[0:n, f % 2, :], scalar=1.0,
                                                       in1=ring[BANK["gate", f]][0:n, :], op0=ALU.add, op1=ALU.mult)\
                                    .then_inc(v_ga, 1)
                            if u == (ENDS["up", f] + 2 if f < GB else ENDS["gate", f] + 2):
                                dve.wait_ge(v_ga, m + 1)
                                if f < GB:
                                    dve.wait_ge(mm["up"], pt * GB + f + 1)
                                if from_tile(pt, 1):
                                    dve.wait_ge(mm["w2"], pt * 2)
                                    dve.wait_ge(mm["down"], pt * 2)
                                up = ring[BANK["gate", f]][64:P, :] if f == GB else ring[BANK["up", f]][:, :]
                                V.tensor_tensor(m5_s[0:64, :] if f == GB else hd_s[:, f, :], th_s[0:n, f % 2, :], up,
                                                ALU.mult).then_inc(v_mh, 1)
                        for f in range(HB):
                            m = pt * HB + f
                            if u == min(ENDS["w1", f] + 2, U - 1):
                                dve.wait_ge(a_ft, m + 1)
                                V.scalar_tensor_tensor(out=th_s[:, f % 2, :], in0=th_s[:, f % 2, :], scalar=1.0,
                                                       in1=ring[BANK["w1", f]][:, :], op0=ALU.add, op1=ALU.mult)\
                                    .then_inc(v_fa, 1)
                            if u == min(ENDS["w3", f] + 2, U - 1):
                                dve.wait_ge(v_fa, m + 1)
                                dve.wait_ge(mm["w3"], m + 1)
                                dve.wait_ge(mm["down"], pt * 2 + 2)
                                V.tensor_tensor(hd_s[:, f, :], th_s[:, f % 2, :], ring[BANK["w3", f]][:, :],
                                                ALU.mult).then_inc(v_hd, 1)

            bodies(dve, body)

        @block.gpsimd
        def _(pool):
            G = nc.gpsimd
            pool.wait_ge(w_zero, 3)

            def body(i, par, pre, units, post):
                nt, pt, other = i + 1, i - 1, 1 - par
                for u in range(U):
                    if units:
                        h = u // UH
                        pool.wait_ge(v_sc, i * U + u + 1)
                        if u % UH == 0:
                            pool.wait_ge(a_c[h], i + 1)
                        if u >= 8 or from_tile(i, 1):
                            pool.wait_ge(pe_y, i * (U // 4) + u // 4 - 1)
                        G.tensor_tensor(hc_s[:, u % 8, :], h_s[:, u % 4, :], c_s[:, h, :], ALU.mult)\
                            .then_inc(g_hc, 1)
                    if pre:
                        if u == 1:
                            pool.wait_ge(v_ve, nt + 1)
                            if from_tile(nt, 1):
                                pool.wait_ge(v_kept, nt)
                                pool.wait_ge(a_u, nt)
                            G.tensor_tensor(rs[:, 0, :], ve[:, 0, :], half_s[:, :], ALU.pow).then_inc(g_rr, 1)
                            pool.wait_ge(g_rr, nt + 1)
                            G.tensor_tensor(mb[:, 0, :], nm[:, 0, :], rs[:, 0, :], ALU.mult).then_inc(g_r, 1)
                        for h in range(2):
                            s0, m = ENDS[f"dtp{h}", 0], nt * 2 + h
                            if u == s0 + 4:
                                pool.wait_ge(v_c, m + 1)
                                G.tensor_tensor(sp_l[:, :], sp_l[:, :], sp_w[:, :], ALU.subtract).then_inc(g_s, 1)
                            if u == s0 + 5:
                                pool.wait_ge(a_rel, m + 1)
                                pool.wait_ge(g_s, m + 1)
                                G.tensor_tensor(sp_l[:, :], sp_l[:, :], sp_r[:, :], ALU.add).then_inc(g_dt, 1)
                            if u == s0 + 7:
                                pool.wait_ge(g_dt, m + 1)
                                pool.wait_ge(l_xrep, (nt + 1) * 128)
                                G.tensor_tensor(sp_w[:, :], sp_l[:, :], xr_s[:, other, h, :], ALU.mult)\
                                    .then_inc(g_dx, 1)
                    if post:
                        if u == ENDS["out", 1] + 2:
                            pool.wait_ge(v_ms, pt + 1)
                            if from_tile(pt, 1):
                                pool.wait_ge(a_hn, pt)
                            G.tensor_tensor(rs[:, 1, 0:SUB], ve[:, 1, 0:SUB], half_s[:, 0:SUB], ALU.pow)\
                                .then_inc(g_r2, 1)
                        for k in range(2):
                            if u == ENDS["out", 1] + 12 + 3 * k:
                                pool.wait_ge(a_hn, pt + 1)
                                pool.wait_ge(l_xo, (pt + 1) * 16)
                                two = slice(2 * k, 2 * k + 2)
                                G.tensor_tensor(res[:, two, :], res[:, two, :], xo[:, two, :], ALU.add)\
                                    .then_inc(g_hx, 1)
                        if u == ENDS["down", 1] + 1:
                            pool.wait_ge(v_ve2, pt + 1)
                            if from_tile(pt, 1):
                                pool.wait_ge(a_xn, pt)
                            G.tensor_tensor(rs[:, 2, 0:SUB], ve[:, 2, 0:SUB], half_s[:, 0:SUB], ALU.pow)\
                                .then_inc(g_rr2, 1)
                            pool.wait_ge(g_rr2, pt + 1)
                            G.tensor_tensor(mb[:, 1, 0:SUB], nm[:, 1, 0:SUB], rs[:, 2, 0:SUB], ALU.mult)\
                                .then_inc(g_r3, 1)
                if post:
                    pool.wait_ge(v_o, pt * 2 + 2)
                    pool.dma_start(rows(out_t, pt), xo[:, :, :]).then_inc(l_out, 16)

            bodies(pool, body)


def kernel(**inputs):
    import numpy as np
    import concourse.bacc as bacc
    from concourse.bass_utils import run_bass_kernel_spmd

    def arr(name):
        return np.asarray(inputs["L0_" + name])

    def blocks(w, cols):
        return w.reshape(-1, P, cols).transpose(1, 0, 2)

    chan = np.arange(D).reshape(2, GH, NS).transpose(0, 2, 1).reshape(-1)
    win = arr("attn_in_proj_w")
    order = np.concatenate([np.arange(640, 768), np.arange(256, 384), np.arange(384, 640), chan])
    gate, up = arr("attn_gate_w").T, arr("attn_up_w").T
    gu = np.concatenate([w[:, f * P:min(f * P + P, FF)] for f in range(GB + 1) for w in (gate, up)], axis=1)
    down = np.zeros(((GB + 1) * P, D), np.float32)
    down[:FF] = arr("attn_down_w").T
    idx = np.arange(P)
    bits = np.array([[bin(a & b).count("1") for b in range(P)] for a in range(P)])
    scale = 1.0 / (2 * H ** 0.5)
    r, c60 = np.arange(P)[:, None], np.arange(60)[None, :]
    data = {
        "x": arr("attn_hidden_states"),
        "in_w": blocks(win[order].T, 768).reshape(P, KD, 6, P),
        "dt_w": arr("attn_dt_proj_w")[chan].T.reshape(P, 2, P),
        "dt_b": arr("attn_dt_proj_b")[chan].reshape(2, P).T,
        "a_log": arr("attn_A_log").reshape(2, GH, NS, NS).transpose(1, 3, 0, 2).reshape(P, U),
        "d_par": arr("attn_D_param")[chan].reshape(2, P).T,
        "out_w": blocks(arr("attn_out_proj_w").T[chan], D),
        "gu_w": blocks(gu, 2 * FF).reshape(P, KD, 2 * GB + 1, P),
        "down_w": blocks(down, D),
        "n1": arr("attn_norm1_w").reshape(KD, P).T,
        "n2": arr("attn_norm2_w").reshape(KD, P).T,
        "w1": blocks(arr("ffn_W1").T, H),
        "w3": blocks(arr("ffn_W3").T, H),
        "w2": blocks(arr("ffn_W2").T, D),
        "ident": np.eye(P, dtype=np.float32),
        "pick": (r % 64 == np.arange(64 * NS)[None, :] // NS).astype(np.float32),
        "ysel": (c60 == 28 + r // NS).astype(np.float32),
        "had": ((1.0 - 2.0 * (bits % 2)) * scale).astype(np.float32),
    }
    nc = bacc.Bacc("TRN2", target_bir_lowering=False, num_devices=1)
    arrays, args = {}, {}
    for name, a in data.items():
        arrays[f"in_{name}"] = np.ascontiguousarray(a)
        args[name] = nc.dram_tensor(f"in_{name}", a.shape, F32, kind="ExternalInput").ap()
    args["out"] = nc.dram_tensor("out_0", (4, SEQ, D), F32, kind="ExternalOutput").ap()
    build(nc, **args)
    res = run_bass_kernel_spmd(nc, [arrays], core_ids=[0])
    return res.results[0]["out_0"]
```
